# Optimizing a Trainium2 kernel written in Bass

```python
import numpy as np
import jax
import jax.numpy as jnp

def _softmax(x, axis=-1):
    return jax.nn.softmax(x, axis=axis)

def _gelu(x):
    return jax.nn.gelu(x, approximate=True)

def _silu(x):
    return jax.nn.silu(x)

def _sigmoid(x):
    return jax.nn.sigmoid(x)

def _layernorm(x, axis=-1, eps=1e-05):
    m = jnp.mean(x, axis=axis, keepdims=True)
    v = jnp.var(x, axis=axis, keepdims=True)
    return (x - m) / jnp.sqrt(v + eps)

def _scatter_add(tgt, idx, src, axis=0):
    return tgt.at[idx].add(src)

def _segment_sum(src, seg, n):
    return jax.ops.segment_sum(src, seg, n)
kernel_name = 'mk_flamingo_gated_d1_seqx_r8_e16fd3'

def setup_inputs(seed: int=0):
    np.random.seed(seed)
    _w = jnp.asarray

    def _rec_inputs():
        import jax
        import jax.numpy as jnp
        _rk = jax.random.key(seed)
        x = -0.0002928 + 1 * jax.random.normal(jax.random.fold_in(_rk, 1), (32, 64, 128), jnp.float32)
        _lenS = 64 - jax.random.randint(jax.random.fold_in(_rk, 7), (32,), 0, max(1, 64 // 4) + 1, jnp.int32)
        _lenS2 = 64 - jax.random.randint(jax.random.fold_in(_rk, 8), (32,), 0, max(1, 64 // 4) + 1, jnp.int32)
        _ctx_1024P = jax.random.normal(jax.random.fold_in(_rk, 11), (32, 16, 128), jnp.float32)
        _ctx_1024c = jax.random.dirichlet(jax.random.fold_in(_rk, 511), 0.3 * jnp.ones((16,), jnp.float32), (32, 64))
        _ctx_1024t = jnp.einsum('bsk,bkd->bsd', _ctx_1024c, _ctx_1024P)
        _ctx_1024t = _ctx_1024t * jax.lax.rsqrt(jnp.mean(jnp.square(_ctx_1024t)) + 1e-12) * 0.953939
        ctx_1024 = 2.81802e-05 + 1.00001 * (_ctx_1024t + 0.3 * jax.random.normal(jax.random.fold_in(_rk, 611), (32, 64, 128), jnp.float32))
        _g = jax.random.normal(jax.random.fold_in(_rk, 9001), (2, 1), jnp.float32)
        _g = jnp.sign(_g) * jnp.maximum(jnp.abs(_g), 1.0) + (_g == 0) * 1.0
        g_xattn = _g[0]
        g_ffn = _g[1]
        return (x, ctx_1024, g_xattn, g_ffn)
    x, ctx_1024, g_xattn, g_ffn = _rec_inputs()

    def _L0_xattn_setup():
        import jax, jax.numpy as jnp
        import numpy as np
        D_MODEL = 128
        N_HEADS = 16
        HEAD_DIM = D_MODEL // N_HEADS
        key = jax.random.key(seed)
        k1, k2, k3, k4, k5, k6 = jax.random.split(key, 6)
        B, T_q, T_kv = (4, 128, 512)
        s = 1.0 / np.sqrt(D_MODEL)
        return {'query': jax.random.normal(k1, (B, T_q, D_MODEL), dtype=jnp.float32), 'kv_source': jax.random.normal(k2, (B, T_kv, D_MODEL), dtype=jnp.float32), 'w_q': jax.random.normal(k3, (D_MODEL, D_MODEL), dtype=jnp.float32) * s, 'w_k': jax.random.normal(k4, (D_MODEL, D_MODEL), dtype=jnp.float32) * s, 'w_v': jax.random.normal(k5, (D_MODEL, D_MODEL), dtype=jnp.float32) * s, 'w_o': jax.random.normal(k6, (D_MODEL, D_MODEL), dtype=jnp.float32) * s}
    _L0_xattn_all = _L0_xattn_setup()
    _L0_xattn_in = {k: v for k, v in _L0_xattn_all.items() if k in ('w_q', 'w_k', 'w_v', 'w_o')}
    del _L0_xattn_all

    def _L0_ffn_setup():
        import jax, jax.numpy as jnp
        import numpy as np
        B, S, D = (2, 128, 128)
        E, K, F, FS = (8, 2, 64, 128)
        key = jax.random.key(seed)
        ks = jax.random.split(key, 9)
        s = lambda k, shape, fan: jax.random.normal(k, shape, jnp.float32) * fan ** (-0.5)
        return {'x': jax.random.normal(ks[0], (B, S, D), jnp.float32), 'Wr': s(ks[1], (D, E), D), 'Wg': s(ks[2], (E, D, F), D), 'Wu': s(ks[3], (E, D, F), D), 'Wd': s(ks[4], (E, F, D), F), 'Sg': s(ks[5], (D, FS), D), 'Su': s(ks[6], (D, FS), D), 'Sd': s(ks[7], (FS, D), FS), 'expert_bias': jnp.zeros((E,), jnp.float32)}
    _L0_ffn_all = _L0_ffn_setup()
    _L0_ffn_in = {k: v for k, v in _L0_ffn_all.items() if k in ('Wr', 'Wg', 'Wu', 'Wd', 'Sg', 'Su', 'Sd', 'expert_bias')}
    del _L0_ffn_all
    return {'x': x, 'ctx_1024': ctx_1024, 'g_xattn': g_xattn, 'g_ffn': g_ffn, 'L0_xattn_w_q': _L0_xattn_in['w_q'], 'L0_xattn_w_k': _L0_xattn_in['w_k'], 'L0_xattn_w_v': _L0_xattn_in['w_v'], 'L0_xattn_w_o': _L0_xattn_in['w_o'], 'L0_ffn_Wr': _L0_ffn_in['Wr'], 'L0_ffn_Wg': _L0_ffn_in['Wg'], 'L0_ffn_Wu': _L0_ffn_in['Wu'], 'L0_ffn_Wd': _L0_ffn_in['Wd'], 'L0_ffn_Sg': _L0_ffn_in['Sg'], 'L0_ffn_Su': _L0_ffn_in['Su'], 'L0_ffn_Sd': _L0_ffn_in['Sd'], 'L0_ffn_expert_bias': _L0_ffn_in['expert_bias']}

def reference(x, ctx_1024, g_xattn, g_ffn, L0_xattn_w_q, L0_xattn_w_k, L0_xattn_w_v, L0_xattn_w_o, L0_ffn_Wr, L0_ffn_Wg, L0_ffn_Wu, L0_ffn_Wd, L0_ffn_Sg, L0_ffn_Su, L0_ffn_Sd, L0_ffn_expert_bias):
    import jax
    import jax.numpy as jnp

    def _L0_xattn_ref(query, kv_source, w_q, w_k, w_v, w_o):
        import jax, jax.numpy as jnp
        import numpy as np
        D_MODEL = 128
        N_HEADS = 16
        HEAD_DIM = D_MODEL // N_HEADS
        B, T_q, _ = query.shape
        T_kv = kv_source.shape[1]
        q = (query @ w_q.T).reshape(B, T_q, N_HEADS, HEAD_DIM)
        k = (kv_source @ w_k.T).reshape(B, T_kv, N_HEADS, HEAD_DIM)
        v = (kv_source @ w_v.T).reshape(B, T_kv, N_HEADS, HEAD_DIM)
        scale = HEAD_DIM ** (-0.5)
        attn = jax.nn.softmax(jnp.einsum('bqhd,bkhd->bhqk', q, k) * scale, axis=-1)
        out = jnp.einsum('bhqk,bkhd->bqhd', attn, v).reshape(B, T_q, D_MODEL)
        return out @ w_o.T

    def _L0_ffn_ref(x, Wr, Wg, Wu, Wd, Sg, Su, Sd, expert_bias):
        import jax, jax.numpy as jnp
        import numpy as np
        B, S, D = (2, 128, 128)
        E, K, F, FS = (8, 2, 64, 128)
        b, s, d = x.shape
        xf = x.reshape(-1, d)
        T = xf.shape[0]
        logits = xf @ Wr + expert_bias
        top_v, top_i = jax.lax.top_k(logits, K)
        probs = jax.nn.softmax(top_v, axis=-1)
        rw = jnp.zeros_like(logits).at[jnp.arange(T)[:, None], top_i].set(probs)
        gate = jnp.einsum('td,edf->tef', xf, Wg)
        up = jnp.einsum('td,edf->tef', xf, Wu)
        h = jax.nn.silu(gate) * up
        eo = jnp.einsum('tef,efd->ted', h, Wd)
        out = jnp.einsum('te,ted->td', rw, eo)
        out = out + jax.nn.silu(xf @ Sg) * (xf @ Su) @ Sd
        return out.reshape(b, s, d)
    x = x + jnp.tanh(g_xattn[0]) * _L0_xattn_ref(_layernorm(x, axis=-1), ctx_1024, L0_xattn_w_q, L0_xattn_w_k, L0_xattn_w_v, L0_xattn_w_o)
    x = x + jnp.tanh(g_ffn[0]) * _L0_ffn_ref(_layernorm(x, axis=-1), L0_ffn_Wr, L0_ffn_Wg, L0_ffn_Wu, L0_ffn_Wd, L0_ffn_Sg, L0_ffn_Su, L0_ffn_Sd, L0_ffn_expert_bias)
    return x

_drawn_inputs = setup_inputs


def setup_inputs(seed=0):
    import zlib

    import numpy as np

    out = dict(_drawn_inputs(seed))
    spreads = {'L0_ffn_expert_bias': (0.0, 0.1)}
    factors = {}
    for name, (base, spread) in spreads.items():
        noise = np.random.default_rng([zlib.crc32(name.encode()), seed]).standard_normal(out[name].shape)
        drawn = base * np.exp(spread * noise) if base else spread * noise
        out[name] = jnp.asarray(drawn.astype(out[name].dtype))
    for name, factor in factors.items():
        out[name] = (out[name] * factor).astype(out[name].dtype)
    return out
```

```python
from contextlib import ExitStack

import concourse.bass as bass
from concourse import mybir

F32 = mybir.dt.float32
U32 = mybir.dt.uint32
ALU = mybir.AluOpType
ACT = mybir.ActivationFunctionType
AX = mybir.AxisListType

P = 128
SEQ = 64
SEQS = P // SEQ
HEADS, HD = 16, 8
PAIRS = HEADS // 2
QUADS = 4
SCALE = HD ** -0.5
EPS = 1e-5
EXPERTS, FE, FS = 8, 64, 128
F0 = 6 * FE
F1 = 2 * FE + FS
FALL = F0 + F1
CHUNKS = FALL // P

C_ID, C_MASK, C_IOTA, C_ONES, C_END = 0, 128, 132, 140, 204
A_Q, A_K, A_V, A_O, A_END = 0, 128, 256, 384, 512
E_G0, E_U0, E_R = 0, F0, 2 * F0
E_G1 = E_R + EXPERTS
E_U1 = E_G1 + F1
E_D = E_U1 + F1
E_END = E_D + CHUNKS * P


def block_kernel(nc, x, ctxT, gates, consts, w_attn, w_ffn, expert_bias, out):
    n_tiles = x.shape[0] // P
    x_tiles = x.rearrange("(t p) d -> p t d", p=P)
    out_tiles = out.rearrange("(t p) d -> t p d", p=P)
    last = n_tiles - 1

    with ExitStack() as stack:
        def sbuf(name, shape, dt=F32):
            return stack.enter_context(nc.sbuf_tensor(name, shape, dt))

        def sem(name):
            return stack.enter_context(nc.semaphore(name))

        cst = sbuf("cst", [P, C_END])
        wa = sbuf("wa", [P, A_END])
        we = sbuf("we", [P, E_END])
        bias = sbuf("bias", [P, EXPERTS])
        g_in = sbuf("g_in", [P, 2])
        g_tanh = sbuf("g_tanh", [P, 2])
        pows = sbuf("pows", [P, 3])
        ident = cst[:, C_ID:C_ID + P]
        head_mask = cst[:, C_MASK:C_MASK + 4]
        iota = cst[:, C_IOTA:C_IOTA + EXPERTS]
        x_all = sbuf("x_all", [P, n_tiles, P])
        ctx = sbuf("ctx", [P, 2, P])
        st1 = sbuf("st1", [P, 6])
        mv1 = sbuf("mv1", [P, 2])
        ve1 = sbuf("ve1", [P, 1])
        rstd1 = sbuf("rstd1", [P, 1])
        xln = sbuf("xln", [P, 2, P])
        xlnT = sbuf("xlnT", [P, P])
        qT = sbuf("qT", [P, 2, P])
        kT = sbuf("kT", [P, P])
        km = sbuf("km", [P, 2, SEQS, 4, SEQ])
        vx = sbuf("vx", [P, 2, SEQS, PAIRS, 32])
        row_max = sbuf("row_max", [P, HEADS])
        probs = sbuf("probs", [P, 2, HEADS, SEQ])
        pT = sbuf("pT", [P, PAIRS, P])
        rden = sbuf("rden", [P, P])
        oT = sbuf("oT", [P, P])
        x1 = sbuf("x1", [P, 2, P])
        st2 = sbuf("st2", [P, 6])
        mv2 = sbuf("mv2", [P, 2])
        ve2 = sbuf("ve2", [P, 1])
        rstd2 = sbuf("rstd2", [P, 1])
        x2ln = sbuf("x2ln", [P, P])
        x2T = sbuf("x2T", [P, P])
        logits = sbuf("logits", [P, EXPERTS])
        top = sbuf("top", [P, 8])
        top_at = sbuf("top_at", [P, 8], U32)
        top_atf = sbuf("top_atf", [P, 8])
        e21 = sbuf("e21", [P, 1])
        den2 = sbuf("den2", [P, 1])
        half_p = sbuf("half_p", [P, 2])
        pick = sbuf("pick", [P, 2, EXPERTS])
        rw = sbuf("rw", [P, EXPERTS + FS // FE])
        th = sbuf("th", [P, FALL])
        sg = sbuf("sg", [P, FALL])
        hu = sbuf("hu", [P, FALL])
        hw = sbuf("hw", [P, FALL])
        hT = sbuf("hT", [P, CHUNKS, P])
        outb = sbuf("outb", [P, 2, P])

        def bank(name):
            return stack.enter_context(nc.psum_tensor(name, [P, 512], F32))

        ps_s = stack.enter_context(nc.psum_tensor("ps_s", [P, HEADS, SEQ], F32))
        ps_t = [bank("ps_t0"), bank("ps_t1")]
        ps_g, ps_u, ps_qkv, ps_o = bank("ps_g"), bank("ps_u"), bank("ps_qkv"), bank("ps_o")
        Q, K, V, XT = (ps_qkv[:, P * i:P * (i + 1)] for i in range(4))
        Y2 = XT
        O, D, Y1, X2T = (ps_o[:, P * i:P * (i + 1)] for i in range(4))

        consts_in, attn_in, x_in, x_rest_in = sem("consts_in"), sem("attn_in"), sem("x_in"), sem("x_rest_in")
        ffn_in, small_in = sem("ffn_in"), sem("small_in")
        ctx_in = [sem("ctx_in0"), sem("ctx_in1")]
        stored = [sem("stored0"), sem("stored1")]
        pows_ready, vx_zeroed, rw_half, gates_ready = sem("pows_ready"), sem("vx_zeroed"), sem("rw_half"), sem("gates_ready")
        st1_done, mv1_ready, rstd1_ready, ve1_done, xln_ready = sem("st1_done"), sem("mv1_ready"), sem("rstd1_ready"), sem("ve1_done"), sem("xln_ready")
        xT_ready, xlnT_ready, qkv_ready = sem("xT_ready"), sem("xlnT_ready"), sem("qkv_ready")
        kT_ready, qT_ready, vx_ready, km_ready = sem("kT_ready"), sem("qT_ready"), sem("vx_ready"), sem("km_ready")
        s_half_done, scores_ready, max_done = sem("s_half_done"), sem("scores_ready"), sem("max_done")
        shifted = [sem("shifted0"), sem("shifted1")]
        probs_ready = [sem("probs_ready0"), sem("probs_ready1")]
        pT_ready = [sem("pT_ready0"), sem("pT_ready1")]
        pT_copied = [sem("pT_copied0"), sem("pT_copied1")]
        pv_ready, rden_done, oT_ready, y1_ready = sem("pv_ready"), sem("rden_done"), sem("oT_ready"), sem("y1_ready")
        x1_done, st2_done, mv2_ready, ve2_done, rstd2_ready = sem("x1_done"), sem("st2_done"), sem("mv2_ready"), sem("ve2_done"), sem("rstd2_ready")
        x2ln_ready, x2T_ready, x2T_copied = sem("x2ln_ready"), sem("x2T_ready"), sem("x2T_copied")
        gu_ready = [sem("gu_ready0"), sem("gu_ready1")]
        th_ready = [sem("th_ready0"), sem("th_ready1")]
        sg_done = [sem("sg_done0"), sem("sg_done1")]
        hu_ready = [sem("hu_ready0"), sem("hu_ready1")]
        hw_ready = [sem("hw_ready0"), sem("hw_ready1")]
        logits_done, top_done, top_ready, e21_ready = sem("logits_done"), sem("top_done"), sem("top_ready"), sem("e21_ready")
        den2_done, p1_done, p2_done = sem("den2_done"), sem("p1_done"), sem("p2_done")
        picked, rw_done = sem("picked"), sem("rw_done")
        hT_ready = [sem("hT_ready0"), sem("hT_ready1")]
        hT_copied = [sem("hT_copied0"), sem("hT_copied1")]
        y2_ready, out_ready = sem("y2_ready"), sem("out_ready")

        block = stack.enter_context(nc.Block())

        def wait(eng, semaphore, value):
            if isinstance(value, int) and value <= 0:
                return
            eng.wait_ge(semaphore, value)

        def wait_apart(eng, semaphore, value, settled):
            if not isinstance(value, int):
                eng.wait_ge(settled, 1)
            wait(eng, semaphore, value)

        def run_steps(eng, step):
            for s in range(-2, 2):
                step(s, s % 2, s)
            with eng.Fori(2, last - 2, 2) as s:
                step(s, 0, 2)
                step(s + 1, 1, 3)
            for s in range(last - 1, last + 3):
                step(s, s % 2, s)

        def exists(t):
            return 0 <= t <= last

        part = [slice(0, F0), slice(F0, FALL)]
        w_g = [we[:, E_G0:E_G0 + F0], we[:, E_G1:E_G1 + F1]]
        w_u = [we[:, E_U0:E_U0 + F0 + EXPERTS], we[:, E_U1:E_U1 + F1]]
        width = [F0, F1]

        @block.sync
        def _(sp):
            sp.dma_start(x_all[:, 0:2, :], x_tiles[:, 0:2, :]).then_inc(x_in, 16)
            sp.dma_start(cst[:], consts).then_inc(consts_in, 16)
            sp.dma_start(wa[:], w_attn).then_inc(attn_in, 16)
            sp.dma_start(x_all[:, 2:, :], x_tiles[:, 2:, :]).then_inc(x_rest_in, 16)

            def step(s, slot, k):
                n, q = s + 1, s - 2
                if exists(k + 1):
                    if k + 1 >= 2:
                        wait(sp, qkv_ready, n - 1)
                    sp.dma_start(ctx[:, 1 - slot, :], ctxT[:, bass.ds(n * P, P)]).then_inc(ctx_in[1 - slot], 16)
                if exists(k - 2):
                    wait(sp, out_ready, q + 1)
                    sp.dma_start(out_tiles[bass.ds(q, 1), :, :].rearrange("o p d -> p (o d)"),
                                 outb[:, slot, :]).then_inc(stored[slot], 16)

            run_steps(sp, step)
            sp.wait_ge(stored[0], 16 * ((n_tiles + 1) // 2))
            sp.wait_ge(stored[1], 16 * (n_tiles // 2))

        @block.scalar
        def _(act):
            act.dma_start(g_in[:], gates.partition_broadcast(P)).then_inc(small_in, 16)
            act.dma_start(bias[:], expert_bias.partition_broadcast(P)).then_inc(small_in, 16)
            act.dma_start(we[:], w_ffn).then_inc(ffn_in, 16)
            act.wait_ge(small_in, 32)
            act.activation(g_tanh[:], g_in[:], ACT.Tanh).then_inc(gates_ready, 1)
            act.wait_ge(vx_zeroed, 1)

            def step(s, slot, k):
                n, a, p, q = s + 1, s, s - 1, s - 2
                if exists(k + 1):
                    wait(act, xT_ready, n + 1)
                    act.copy(xlnT[:], XT).then_inc(xlnT_ready, 1)
                    wait(act, qkv_ready, n + 1)
                    wait(act, km_ready, n)
                    act.copy(kT[:], K).then_inc(kT_ready, 1)
                    act.copy(qT[:, 1 - slot, :], Q).then_inc(qT_ready, 1)
                    for h2 in range(2):
                        rows = slice(SEQ * h2, SEQ * (h2 + 1))
                        dst = vx[rows, 1 - slot, :, :, :].rearrange("p b (g c) (e d) -> p (b g) c e d", c=2, e=4)
                        src = V[rows, :].rearrange("p (bg c d) -> p bg c d", c=2, d=HD)
                        for c in range(2):
                            v_copy = act.copy(dst[:, :, c, 2 * c + h2, :], src[:, :, c, :])
                    v_copy.then_inc(vx_ready, 1)
                if exists(k - 2):
                    for f, chunks in ((0, range(3)), (1, range(3, CHUNKS))):
                        wait(act, hT_ready[f], q + 1)
                        w = len(chunks) * P
                        act.copy(hT[:, chunks[0]:chunks[-1] + 1, :], ps_t[f][:, 0:w].rearrange("p (c t) -> p c t", t=P)) \
                           .then_inc(hT_copied[f], 1)
                if exists(k - 1):
                    wait(act, x2T_ready, p + 1)
                    act.copy(x2T[:], X2T).then_inc(x2T_copied, 1)
                if exists(k):
                    for c in range(2):
                        wait(act, shifted[c], a + 1)
                        half = probs[:, slot, 8 * c:8 * c + 8, :]
                        act.activation(half, half, ACT.Exp, scale=SCALE).then_inc(probs_ready[c], 1)
                    wait(act, pT_ready[0], a + 1)
                    act.copy(pT[:, 0:4, :], ps_t[0][:].rearrange("p (c t) -> p c t", t=P)).then_inc(pT_copied[0], 1)
                if exists(k - 1):
                    wait(act, gu_ready[0], p + 1)
                    act.activation(th[:, part[0]], ps_g[:, 0:F0], ACT.Tanh, scale=0.5).then_inc(th_ready[0], 1)
                if exists(k):
                    wait(act, pT_ready[1], a + 1)
                    act.copy(pT[:, 4:8, :], ps_t[1][:].rearrange("p (c t) -> p c t", t=P)).then_inc(pT_copied[1], 1)
                if exists(k - 1):
                    wait(act, top_ready, p + 1)
                    act.activation(e21[:], top[:, 0:1], ACT.Exp, bias=top[:, 1:2], scale=-1.0).then_inc(e21_ready, 1)
                    wait(act, gu_ready[1], p + 1)
                    act.activation(th[:, part[1]], ps_g[:, 0:F1], ACT.Tanh, scale=0.5).then_inc(th_ready[1], 1)

            run_steps(act, step)

        @block.gpsimd
        def _(pool):
            pool.memset(pows[:, 0:1], -0.5)
            pool.memset(pows[:, 2:3], EPS)
            pool.memset(pows[:, 1:2], -1.0).then_inc(pows_ready, 1)
            pool.memset(rw[:], 0.5).then_inc(rw_half, 1)
            pool.wait_ge(pows_ready, 1)
            pool.wait_ge(rw_half, 1)
            pool.wait_ge(consts_in, 16)

            def inverse_root(t, mv, ve, rstd, mv_ready, ve_done, rstd_ready):
                wait(pool, mv_ready, t + 1)
                pool.tensor_tensor(ve[:], mv[:, 1:2], pows[:, 2:3], ALU.add).then_inc(ve_done, 1)
                wait(pool, ve_done, t + 1)
                pool.tensor_tensor(rstd[:], ve[:], pows[:, 0:1], ALU.pow).then_inc(rstd_ready, 1)

            def step(s, slot, k):
                m, n, p = s + 2, s + 1, s - 1
                if exists(k - 1):
                    inverse_root(p, mv2, ve2, rstd2, mv2_ready, ve2_done, rstd2_ready)
                if exists(k + 2):
                    inverse_root(m, mv1, ve1, rstd1, mv1_ready, ve1_done, rstd1_ready)
                if exists(k + 1):
                    wait(pool, kT_ready, n + 1)
                    keys = kT[:].rearrange("p (b o k) -> p b o k", b=SEQS, o=1).broadcast_to([P, SEQS, 4, SEQ])
                    mask = head_mask.rearrange("p (o j u) -> p o j u", o=1, u=1).broadcast_to([P, SEQS, 4, SEQ])
                    pool.tensor_tensor(km[:, 1 - slot, :, :, :], keys, mask, ALU.mult).then_inc(km_ready, 1)
                if exists(k - 1):
                    wait_apart(pool, top_ready, p + 1, pows_ready)
                    pool.tensor_copy(top_atf[:], top_at[:])
                    wait_apart(pool, e21_ready, p + 1, pows_ready)
                    pool.tensor_scalar(den2[:], e21[:], 2.0, 2.0, ALU.mult, ALU.add).then_inc(den2_done, 1)
                    wait(pool, den2_done, p + 1)
                    pool.tensor_tensor(half_p[:, 0:1], den2[:], pows[:, 1:2], ALU.pow).then_inc(p1_done, 1)
                    wait(pool, p1_done, p + 1)
                    pool.tensor_tensor(half_p[:, 1:2], e21[:], half_p[:, 0:1], ALU.mult).then_inc(p2_done, 1)
                    wait_apart(pool, p2_done, p + 1, pows_ready)
                    for i in range(2):
                        pick_i = pool.tensor_scalar(pick[:, i, :], iota, top_atf[:, i:i + 1], half_p[:, i:i + 1],
                                                    ALU.is_equal, ALU.mult)
                    pick_i.then_inc(picked, 1)
                    wait(pool, picked, p + 1)
                    pool.tensor_tensor(rw[:, 0:EXPERTS], pick[:, 0, :], pick[:, 1, :], ALU.add).then_inc(rw_done, 1)
                    wait(pool, rw_done, p + 1)
                    for f in range(2):
                        wait(pool, hu_ready[f], p + 1)
                        e0, e1 = part[f].start // FE, part[f].stop // FE
                        pool.tensor_tensor(hw[:, part[f]].rearrange("p (e f) -> p e f", f=FE),
                                           hu[:, part[f]].rearrange("p (e f) -> p e f", f=FE),
                                           rw[:, e0:e1].rearrange("p (e o) -> p e o", o=1).broadcast_to([P, e1 - e0, FE]),
                                           ALU.mult).then_inc(hw_ready[f], 1)

            run_steps(pool, step)

        @block.vector
        def _(dve):
            dve.memset(vx[:], 0.0).then_inc(vx_zeroed, 1)
            dve.wait_ge(x_in, 16)
            dve.wait_ge(gates_ready, 1)

            def gated_part(f, p):
                dve.scalar_tensor_tensor(sg[:, part[f]], th[:, part[f]], 1.0, ps_g[:, 0:width[f]], ALU.add, ALU.mult) \
                   .then_inc(sg_done[f], 1)

            def up_part(f, p):
                wait(dve, sg_done[f], p + 1)
                dve.tensor_tensor(hu[:, part[f]], sg[:, part[f]], ps_u[:, 0:width[f]], ALU.mult).then_inc(hu_ready[f], 1)

            def step(s, slot, k):
                m, a, p, q = s + 2, s, s - 1, s - 2
                if exists(k + 2):
                    if k == 0:
                        dve.wait_ge(x_rest_in, 16)
                    x_m = x_all[:, bass.ds(m, 1), :].rearrange("p o d -> p (o d)")
                    dve.bn_stats(st1[:], x_m).then_inc(st1_done, 1)
                if exists(k - 1):
                    wait(dve, y1_ready, p + 1)
                    dve.scalar_tensor_tensor(x1[:, 1 - slot, :], Y1, g_tanh[:, 0:1],
                                             x_all[:, bass.ds(p, 1), :].rearrange("p o d -> p (o d)"),
                                             ALU.mult, ALU.add).then_inc(x1_done, 1)
                    wait(dve, x1_done, p + 1)
                    dve.bn_stats(st2[:], x1[:, 1 - slot, :]).then_inc(st2_done, 1)
                    wait_apart(dve, st2_done, p + 1, gates_ready)
                    dve.bn_aggr(mv2[:], st2[:]).then_inc(mv2_ready, 1)
                if exists(k + 2):
                    if not exists(k - 1):
                        dve.wait_ge(st1_done, k + 3)
                    dve.bn_aggr(mv1[:], st1[:]).then_inc(mv1_ready, 1)
                if exists(k - 1):
                    wait(dve, rstd2_ready, p + 1)
                    dve.tensor_scalar(x2ln[:], x1[:, 1 - slot, :], mv2[:, 0:1], rstd2[:, 0:1], ALU.subtract, ALU.mult) \
                       .then_inc(x2ln_ready, 1)
                if exists(k):
                    wait(dve, scores_ready, a + 1)
                    dve.tensor_reduce(row_max[:], ps_s[:], AX.X, ALU.max).then_inc(max_done, 1)
                    wait(dve, max_done, a + 1)
                    for c in range(2):
                        heads = slice(8 * c, 8 * c + 8)
                        dve.tensor_tensor(probs[:, slot, heads, :], ps_s[:, heads, :],
                                          row_max[:, heads].rearrange("p (h o) -> p h o", o=1).broadcast_to([P, 8, SEQ]),
                                          ALU.subtract).then_inc(shifted[c], 1)
                if exists(k - 2):
                    wait(dve, y2_ready, q + 1)
                    if k - 2 >= 2:
                        wait(dve, stored[slot], (q - (k % 2)) * 8)
                    dve.scalar_tensor_tensor(outb[:, slot, :], Y2, g_tanh[:, 1:2], x1[:, slot, :],
                                             ALU.mult, ALU.add).then_inc(out_ready, 1)
                if exists(k + 2):
                    wait(dve, rstd1_ready, m + 1)
                    dve.tensor_scalar(xln[:, slot, :], x_m, mv1[:, 0:1], rstd1[:, 0:1], ALU.subtract, ALU.mult) \
                       .then_inc(xln_ready, 1)
                if exists(k - 1):
                    if k == 1:
                        dve.wait_ge(small_in, 32)
                    wait(dve, th_ready[0], p + 1)
                    dve.tensor_tensor(logits[:], ps_u[:, F0:F0 + EXPERTS], bias[:], ALU.add).then_inc(logits_done, 1)
                    gated_part(0, p)
                    wait_apart(dve, logits_done, p + 1, gates_ready)
                    dve.max(top[:], logits[:]).then_inc(top_done, 1)
                    up_part(0, p)
                    wait_apart(dve, top_done, p + 1, gates_ready)
                    dve.max_index(top_at[:], top[:], logits[:]).then_inc(top_ready, 1)
                if exists(k):
                    wait(dve, pv_ready, a + 1)
                    dve.reciprocal(rden[:], D).then_inc(rden_done, 1)
                    wait(dve, rden_done, a + 1)
                    dve.tensor_tensor(oT[:], O, rden[:], ALU.mult).then_inc(oT_ready, 1)
                if exists(k - 1):
                    wait(dve, th_ready[1], p + 1)
                    gated_part(1, p)
                    up_part(1, p)

            run_steps(dve, step)

        @block.tensor
        def _(pe):
            def scores(a, slot, half):
                for b in range(SEQS):
                    for quad in (half, half + 2):
                        rows = slice(32 * quad, 32 * quad + 32)
                        cols = slice(SEQ * b, SEQ * (b + 1))
                        mm = pe.matmul(ps_s[cols, 4 * quad:4 * quad + 4, :], qT[rows, slot, cols], km[rows, slot, b, :, :],
                                       start=True, stop=True, tile_position=(32 * quad, SEQ * b))
                return mm

            def step(s, slot, k):
                n, a, p, q = s + 1, s, s - 1, s - 2
                if exists(k + 1):
                    if k + 1 == 0:
                        pe.wait_ge(consts_in, 16)
                        pe.wait_ge(attn_in, 16)
                    wait(pe, xln_ready, n + 1)
                    if k - 3 >= 0:
                        wait(pe, out_ready, q)
                    wait(pe, vx_ready, n)
                    pe.transpose(XT, xln[:, 1 - slot, :], ident).then_inc(xT_ready, 1)
                if exists(k):
                    wait(pe, shifted[1], a)
                    wait(pe, km_ready, a + 1)
                    wait(pe, qT_ready, a + 1)
                    scores(a, slot, 0).then_inc(s_half_done, 1)
                if exists(k - 1):
                    wait(pe, oT_ready, p + 1)
                    pe.matmul(Y1, oT[:], wa[:, A_O:A_O + P], start=True, stop=True).then_inc(y1_ready, 1)
                if exists(k + 1):
                    wait(pe, ctx_in[1 - slot], (n - ((k + 1) % 2)) * 8 + 16)
                    wait(pe, xlnT_ready, n + 1)
                    pe.matmul(K, wa[:, A_K:A_K + P], ctx[:, 1 - slot, :], start=True, stop=True)
                    pe.matmul(Q, wa[:, A_Q:A_Q + P], xlnT[:], start=True, stop=True)
                    for b in range(SEQS):
                        for h2 in range(2):
                            mm = pe.matmul(V[SEQ * h2:SEQ * (h2 + 1), SEQ * b:SEQ * (b + 1)],
                                           ctx[:, 1 - slot, SEQ * b:SEQ * (b + 1)],
                                           wa[:, A_V + SEQ * h2:A_V + SEQ * (h2 + 1)],
                                           start=True, stop=True, tile_position=(0, SEQ * h2))
                    mm.then_inc(qkv_ready, 1)
                if exists(k - 2):
                    for f, chunks in ((0, range(3)), (1, range(3, CHUNKS))):
                        wait(pe, hw_ready[f], q + 1)
                        wait(pe, pT_copied[f], q + 2 if k <= last + 1 else last + 1)
                        for i, c in enumerate(chunks):
                            mm = pe.transpose(ps_t[f][:, P * i:P * (i + 1)], hw[:, P * c:P * (c + 1)], ident)
                        mm.then_inc(hT_ready[f], 1)
                if exists(k):
                    wait(pe, s_half_done, a + 1)
                    scores(a, slot, 1).then_inc(scores_ready, 1)
                if exists(k - 1):
                    wait(pe, x2ln_ready, p + 1)
                    pe.transpose(X2T, x2ln[:], ident).then_inc(x2T_ready, 1)
                if exists(k - 2):
                    if exists(k + 1):
                        wait(pe, vx_ready, n + 1)
                    for f, chunks in ((0, range(3)), (1, range(3, CHUNKS))):
                        wait(pe, hT_copied[f], q + 1)
                        for c in chunks:
                            mm = pe.matmul(Y2, hT[:, c, :], we[:, E_D + P * c:E_D + P * (c + 1)],
                                           start=(c == 0), stop=(c == CHUNKS - 1))
                    mm.then_inc(y2_ready, 1)

                def gate_up(f):
                    pe.matmul(ps_g[:, 0:width[f]], x2T[:], w_g[f], start=True, stop=True)
                    n_u = w_u[f].shape[1]
                    pe.matmul(ps_u[:, 0:n_u], x2T[:], w_u[f], start=True, stop=True).then_inc(gu_ready[f], 1)

                if exists(k - 1):
                    if k == 1:
                        pe.wait_ge(ffn_in, 16)
                    wait(pe, x2T_copied, p + 1)
                    wait(pe, hu_ready[1], p)
                    gate_up(0)
                if exists(k):
                    for c in range(2):
                        wait(pe, probs_ready[c], a + 1)
                        wait(pe, hT_copied[c], q + 1)
                        for i in range(4):
                            h = 8 * c + 2 * i
                            mm = pe.transpose(ps_t[c][:, P * i:P * (i + 1)],
                                              probs[:, slot, h:h + 2, :].rearrange("p h k -> p (h k)"), ident)
                        mm.then_inc(pT_ready[c], 1)
                    wait(pe, pT_copied[0], a + 1)
                    wait(pe, pT_copied[1], a + 1)
                    for b in range(SEQS):
                        cols = slice(SEQ * b, SEQ * (b + 1))
                        for c in range(2):
                            for quad in range(QUADS):
                                pair = 2 * quad + c
                                pe.matmul(O[32 * quad:32 * quad + 32, cols], vx[:, slot, b, pair, :], pT[:, pair, cols],
                                          start=(c == 0), stop=(c == 1), tile_position=(0, 32 * quad))
                    for c in range(2):
                        for quad in range(QUADS):
                            pair = 2 * quad + c
                            mm = pe.matmul(D[32 * quad:32 * quad + 32, :], cst[:, C_ONES + 32 * c:C_ONES + 32 * (c + 1)],
                                           pT[:, pair, :], start=(c == 0), stop=(c == 1), tile_position=(0, 32 * quad))
                    mm.then_inc(pv_ready, 1)
                if exists(k - 1):
                    wait(pe, hu_ready[0], p + 1)
                    gate_up(1)

            run_steps(pe, step)


def kernel(x, ctx_1024, g_xattn, g_ffn, L0_xattn_w_q, L0_xattn_w_k, L0_xattn_w_v, L0_xattn_w_o, L0_ffn_Wr,
           L0_ffn_Wg, L0_ffn_Wu, L0_ffn_Wd, L0_ffn_Sg, L0_ffn_Su, L0_ffn_Sd, L0_ffn_expert_bias):
    import numpy as np
    import concourse.bacc as bacc
    from concourse.bass_utils import run_bass_kernel_spmd

    shape = x.shape
    rows = shape[0] * shape[1]

    consts = np.zeros((P, C_END), np.float32)
    r = np.arange(P)
    consts[r, C_ID + r] = 1
    consts[r, C_MASK + r % 32 // HD] = 1
    consts[:, C_IOTA:C_IOTA + EXPERTS] = np.arange(EXPERTS)
    for c in range(2):
        for d in range(HD):
            consts[r, C_ONES + 32 * c + 16 * c + HD * (r // SEQ) + d] = 1

    wv = np.asarray(L0_xattn_w_v).reshape(PAIRS, 2, HD, P).transpose(1, 0, 2, 3).reshape(P, P)
    w_attn = np.concatenate([np.asarray(L0_xattn_w_q).T, np.asarray(L0_xattn_w_k).T, wv.T, np.asarray(L0_xattn_w_o).T], axis=1)

    def features(w, shared):
        return np.concatenate([np.asarray(w).transpose(1, 0, 2).reshape(P, EXPERTS * FE), np.asarray(shared)], axis=1)

    wg, wu = features(L0_ffn_Wg, L0_ffn_Sg), features(L0_ffn_Wu, L0_ffn_Su)
    wd = np.concatenate([np.asarray(L0_ffn_Wd).reshape(EXPERTS * FE, P), np.asarray(L0_ffn_Sd)], axis=0)
    wd = wd.reshape(CHUNKS, P, P).transpose(1, 0, 2).reshape(P, CHUNKS * P)
    w_ffn = np.concatenate([wg[:, :F0], wu[:, :F0], np.asarray(L0_ffn_Wr), wg[:, F0:], wu[:, F0:], wd], axis=1)

    arrays = {
        "x": np.asarray(x).reshape(rows, P),
        "ctxT": np.asarray(ctx_1024).reshape(rows, P).T,
        "gates": np.concatenate([np.asarray(g_xattn), np.asarray(g_ffn)]),
        "consts": consts,
        "w_attn": w_attn,
        "w_ffn": w_ffn,
        "expert_bias": np.asarray(L0_ffn_expert_bias),
    }
    arrays = {k: np.ascontiguousarray(v) for k, v in arrays.items()}
    nc = bacc.Bacc("TRN2", target_bir_lowering=False, num_devices=1)
    args = [nc.dram_tensor(k, v.shape, mybir.dt.from_np(v.dtype), kind="ExternalInput").ap() for k, v in arrays.items()]
    out = nc.dram_tensor("out", (rows, P), F32, kind="ExternalOutput").ap()
    block_kernel(nc, *args, out)
    got = run_bass_kernel_spmd(nc, [arrays], core_ids=[0])
    return got.results[0]["out"].reshape(shape)
```

```python
from contextlib import ExitStack

import concourse.bass as bass
from concourse import mybir

F32 = mybir.dt.float32
F32R = mybir.dt.float32r
U32 = mybir.dt.uint32
ALU = mybir.AluOpType
ACT = mybir.ActivationFunctionType
AX = mybir.AxisListType

P = 128
SEQ = 64
SEQS = P // SEQ
HEADS, HD = 16, 8
PAIRS = HEADS // 2
QUADS = 4
SCALE = HD ** -0.5
EPS = 1e-5
EXPERTS, FE, FS = 8, 64, 128
F0 = 6 * FE
F1 = 2 * FE + FS
FALL = F0 + F1
CHUNKS = FALL // P
WARM = [9, 5, 1, 7, 3, 5, 10, 2]

C_ID, C_MASK, C_IOTA, C_ONES, C_END = 0, 128, 132, 140, 204
A_Q, A_K, A_V, A_O, A_END = 0, 128, 256, 384, 512
E_G0, E_U0, E_R = 0, F0, 2 * F0
E_G1 = E_R + EXPERTS
E_U1 = E_G1 + F1
E_D = E_U1 + F1
E_END = E_D + CHUNKS * P


def block_kernel(nc, x, ctxT, gates, consts, w_attn, w_ffn, expert_bias, out):
    n_tiles = x.shape[0] // P
    x_tiles = x.rearrange("(t p) d -> p t d", p=P)
    out_tiles = out.rearrange("(t p) d -> t p d", p=P)
    last = n_tiles - 1

    with ExitStack() as stack:
        def sbuf(name, shape, dt=F32):
            return stack.enter_context(nc.sbuf_tensor(name, shape, dt))

        def sem(name):
            return stack.enter_context(nc.semaphore(name))

        cst = sbuf("cst", [P, C_END])
        wa = sbuf("wa", [P, A_END])
        we = sbuf("we", [P, E_END])
        we_hi = sbuf("we_hi", [P, E_D], F32R)
        we_lo = sbuf("we_lo", [P, E_D], F32R)
        bias = sbuf("bias", [P, EXPERTS])
        g_in = sbuf("g_in", [P, 2])
        g_tanh = sbuf("g_tanh", [P, 2])
        zeros = sbuf("zeros", [P, P])
        pows = sbuf("pows", [P, 3])
        ident = cst[:, C_ID:C_ID + P]
        head_mask = cst[:, C_MASK:C_MASK + 4]
        iota = cst[:, C_IOTA:C_IOTA + EXPERTS]
        x_all = sbuf("x_all", [P, n_tiles, P])
        ctx = sbuf("ctx", [P, 2, P])
        st1 = sbuf("st1", [P, 6])
        mv1 = sbuf("mv1", [P, 2])
        ve1 = sbuf("ve1", [P, 1])
        rstd1 = sbuf("rstd1", [P, 1])
        xln = sbuf("xln", [P, 2, P])
        xlnT = sbuf("xlnT", [P, P])
        qT = sbuf("qT", [P, 2, P])
        kT = sbuf("kT", [P, P])
        km = sbuf("km", [P, 2, SEQS, 4, SEQ])
        vx = sbuf("vx", [P, 2, SEQS * QUADS, 2, 48])
        row_max = sbuf("row_max", [P, HEADS])
        probs = sbuf("probs", [P, 2, HEADS, SEQ])
        pT = sbuf("pT", [P, PAIRS, P])
        rden = sbuf("rden", [P, P])
        oT = sbuf("oT", [P, P])
        x1 = sbuf("x1", [P, 2, P])
        st2 = sbuf("st2", [P, 6])
        mv2 = sbuf("mv2", [P, 2])
        ve2 = sbuf("ve2", [P, 1])
        rstd2 = sbuf("rstd2", [P, 1])
        x2ln = sbuf("x2ln", [P, P])
        x2h = sbuf("x2h", [P, P], F32R)
        x2l = sbuf("x2l", [P, P], F32R)
        logits = sbuf("logits", [P, EXPERTS])
        top = sbuf("top", [P, 8])
        top_at = sbuf("top_at", [P, 8], U32)
        top_atf = sbuf("top_atf", [P, 8])
        e21 = sbuf("e21", [P, 1])
        den2 = sbuf("den2", [P, 1])
        half_p = sbuf("half_p", [P, 2])
        pick = sbuf("pick", [P, 2, EXPERTS])
        rw = sbuf("rw", [P, EXPERTS + FS // FE])
        th = sbuf("th", [P, FALL])
        sg = sbuf("sg", [P, FALL])
        hu = sbuf("hu", [P, FALL])
        hw = sbuf("hw", [P, FALL])
        hT = sbuf("hT", [P, CHUNKS, P])
        outb = sbuf("outb", [P, 2, P])

        def bank(name):
            return stack.enter_context(nc.psum_tensor(name, [P, 512], F32))

        ps_s = stack.enter_context(nc.psum_tensor("ps_s", [P, HEADS, SEQ], F32))
        ps_t = [bank("ps_t0"), bank("ps_t1")]
        ps_g, ps_u, ps_qkv, ps_o = bank("ps_g"), bank("ps_u"), bank("ps_qkv"), bank("ps_o")
        Q, K, V, XT = (ps_qkv[:, P * i:P * (i + 1)] for i in range(4))
        X2T = XT
        O, Y2, Y1, _ = (ps_o[:, P * i:P * (i + 1)] for i in range(4))
        D = ps_t[0][:, 0:P]

        consts_in, attn_in = sem("consts_in"), sem("attn_in")
        x_in, x_next_in, x_rest_in = sem("x_in"), sem("x_next_in"), sem("x_rest_in")
        ffn_in, small_in = sem("ffn_in"), sem("small_in")
        ctx_in = [sem("ctx_in0"), sem("ctx_in1")]
        stored = [sem("stored0"), sem("stored1")]
        zeros_set = sem("zeros_set")
        we_hi_ready, we_lo_ready = sem("we_hi_ready"), sem("we_lo_ready")
        pows_ready, vx_zeroed, rw_half, gates_ready = sem("pows_ready"), sem("vx_zeroed"), sem("rw_half"), sem("gates_ready")
        st1_done, mv1_ready, rstd1_ready, ve1_done, xln_ready = sem("st1_done"), sem("mv1_ready"), sem("rstd1_ready"), sem("ve1_done"), sem("xln_ready")
        xT_ready, xlnT_ready, qkv_ready = sem("xT_ready"), sem("xlnT_ready"), sem("qkv_ready")
        kT_ready, qT_ready, vx_ready, km_ready = sem("kT_ready"), sem("qT_ready"), sem("vx_ready"), sem("km_ready")
        s_half_done, scores_ready = sem("s_half_done"), sem("scores_ready")
        max_done = [sem("max_done0"), sem("max_done1")]
        shifted = [sem("shifted0"), sem("shifted1")]
        probs_ready = [sem("probs_ready0"), sem("probs_ready1")]
        pT_ready = [sem("pT_ready0"), sem("pT_ready1")]
        pT_copied = [sem("pT_copied0"), sem("pT_copied1")]
        den_ready, rden_done, pv_ready, oT_ready, y1_ready = sem("den_ready"), sem("rden_done"), sem("pv_ready"), sem("oT_ready"), sem("y1_ready")
        x1_done, st2_done, mv2_ready, ve2_done, rstd2_ready = sem("x1_done"), sem("st2_done"), sem("mv2_ready"), sem("ve2_done"), sem("rstd2_ready")
        x2ln_ready, x2T_ready, x2h_ready, x2l_ready = sem("x2ln_ready"), sem("x2T_ready"), sem("x2h_ready"), sem("x2l_ready")
        g_ready = [sem("g_ready0"), sem("g_ready1")]
        u_ready = [sem("u_ready0"), sem("u_ready1")]
        th_ready = [sem("th_ready0"), sem("th_ready1")]
        sg_done = [sem("sg_done0"), sem("sg_done1")]
        hu_ready = [sem("hu_ready0"), sem("hu_ready1")]
        hw_ready = [sem("hw_ready0"), sem("hw_ready1")]
        logits_done, top_done, top_ready, e21_ready = sem("logits_done"), sem("top_done"), sem("top_ready"), sem("e21_ready")
        den2_done, p1_done, p2_done = sem("den2_done"), sem("p1_done"), sem("p2_done")
        picked, rw_done = sem("picked"), sem("rw_done")
        hT_ready = [sem("hT_ready0"), sem("hT_ready1")]
        hT_copied = [sem("hT_copied0"), sem("hT_copied1")]
        y2_ready, out_ready = sem("y2_ready"), sem("out_ready")

        block = stack.enter_context(nc.Block())

        def wait(eng, semaphore, value):
            if isinstance(value, int) and value <= 0:
                return
            eng.wait_ge(semaphore, value)

        def wait_apart(eng, semaphore, value, settled):
            if not isinstance(value, int):
                eng.wait_ge(settled, 1)
            wait(eng, semaphore, value)

        def run_steps(eng, step):
            for s in range(-2, 2):
                step(s, s % 2, s)
            with eng.Fori(2, last - 2, 2) as s:
                step(s, 0, 2)
                step(s + 1, 1, 3)
            for s in range(last - 1, last + 3):
                step(s, s % 2, s)

        def exists(t):
            return 0 <= t <= last

        part = [slice(0, F0), slice(F0, FALL)]
        g_cols = [slice(E_G0, E_G0 + F0), slice(E_G1, E_G1 + F1)]
        u_cols = [slice(E_U0, E_U0 + F0 + EXPERTS), slice(E_U1, E_U1 + F1)]
        width = [F0, F1]

        def gu_banks(f, k):
            if f == 1 and k == last + 1:
                flat = ps_s[:].rearrange("p h k -> p (h k)")
                return flat[:, 0:512], flat[:, 512:1024]
            return ps_g, ps_u

        def v_window(slot, b, pair):
            c = pair % 2
            return vx[:, slot, QUADS * b + pair // 2, :, :].rearrange("p c w -> p (c w)")[:, 32 * c:32 * c + 32]

        @block.sync
        def _(sp):
            sp.dma_start(x_all[:, 0:2, :], x_tiles[:, 0:2, :]).then_inc(x_in, 16)
            sp.dma_start(wa[:], w_attn).then_inc(attn_in, 16)
            for n in range(2):
                sp.dma_start(ctx[:, n, :], ctxT[:, P * n:P * (n + 1)]).then_inc(ctx_in[n], 16)
            sp.dma_start(x_all[:, 2:4, :], x_tiles[:, 2:4, :]).then_inc(x_next_in, 16)
            sp.dma_start(x_all[:, 4:, :], x_tiles[:, 4:, :]).then_inc(x_rest_in, 16)

            def step(s, slot, k):
                n, q = s + 1, s - 2
                if exists(k + 1) and k + 1 >= 2:
                    wait(sp, qkv_ready, n - 1)
                    sp.dma_start(ctx[:, 1 - slot, :], ctxT[:, bass.ds(n * P, P)]).then_inc(ctx_in[1 - slot], 16)
                if exists(k - 2):
                    wait(sp, out_ready, q + 1)
                    sp.dma_start(out_tiles[bass.ds(q, 1), :, :].rearrange("o p d -> p (o d)"),
                                 outb[:, slot, :]).then_inc(stored[slot], 16)

            run_steps(sp, step)
            sp.wait_ge(stored[0], 16 * ((n_tiles + 1) // 2))
            sp.wait_ge(stored[1], 16 * (n_tiles // 2))

        @block.scalar
        def _(act):
            act.dma_start(cst[:], consts).then_inc(consts_in, 16)
            act.dma_start(g_in[:], gates.partition_broadcast(P)).then_inc(small_in, 16)
            act.dma_start(bias[:], expert_bias.partition_broadcast(P)).then_inc(small_in, 16)
            act.dma_start(we[:], w_ffn).then_inc(ffn_in, 16)
            act.wait_ge(small_in, 32)
            act.activation(g_tanh[:], g_in[:], ACT.Tanh).then_inc(gates_ready, 1)
            act.wait_ge(vx_zeroed, 1)

            def step(s, slot, k):
                m, n, a, p, q = s + 2, s + 1, s, s - 1, s - 2
                hT_parts = ((0, range(3)), (1, range(3, CHUNKS)))

                def copy_hT(f, chunks):
                    wait(act, hT_ready[f], q + 1)
                    act.copy(hT[:, chunks[0]:chunks[-1] + 1, :],
                             ps_t[f][:, 0:len(chunks) * P].rearrange("p (c t) -> p c t", t=P)).then_inc(hT_copied[f], 1)

                def exponentials(c):
                    wait(act, shifted[c], a + 1)
                    half = probs[:, slot, 8 * c:8 * c + 8, :]
                    act.activation(half, half, ACT.Exp, scale=SCALE).then_inc(probs_ready[c], 1)

                def copy_pT(c):
                    wait(act, pT_ready[c], a + 1)
                    act.copy(pT[:, 4 * c:4 * c + 4, :], ps_t[c][:].rearrange("p (c t) -> p c t", t=P)).then_inc(pT_copied[c], 1)

                if exists(k - 2):
                    copy_hT(*hT_parts[0])
                if exists(k + 1):
                    wait(act, qkv_ready, n + 1)
                    wait(act, km_ready, n)
                    act.copy(kT[:], K).then_inc(kT_ready, 1)
                    act.copy(qT[:, 1 - slot, :], Q).then_inc(qT_ready, 1)
                    for h2 in range(2):
                        rows = slice(SEQ * h2, SEQ * (h2 + 1))
                        v_copy = act.copy(vx[rows, 1 - slot, :, :, HD * h2:HD * (h2 + 1)],
                                          V[rows, :].rearrange("p (bg c d) -> p bg c d", c=2, d=HD))
                    v_copy.then_inc(vx_ready, 1)
                if exists(k - 2):
                    copy_hT(*hT_parts[1])
                if exists(k):
                    exponentials(0)
                if exists(k - 1):
                    wait(act, x2T_ready, p + 1)
                    act.copy(x2h[:], X2T).then_inc(x2h_ready, 1)
                if k == 0:
                    exponentials(1)
                    copy_pT(0)
                elif exists(k):
                    copy_pT(0)
                    exponentials(1)
                if exists(k - 1):
                    wait(act, g_ready[0], p + 1)
                    act.activation(th[:, part[0]], ps_g[:, 0:F0], ACT.Tanh, scale=0.5).then_inc(th_ready[0], 1)
                    wait(act, top_ready, p + 1)
                    act.activation(e21[:], top[:, 0:1], ACT.Exp, bias=top[:, 1:2], scale=-1.0).then_inc(e21_ready, 1)
                if exists(k):
                    copy_pT(1)
                if exists(k - 1):
                    wait(act, g_ready[1], p + 1)
                    act.activation(th[:, part[1]], gu_banks(1, k)[0][:, 0:F1], ACT.Tanh, scale=0.5).then_inc(th_ready[1], 1)
                if exists(k + 2):
                    wait(act, xT_ready, m + 1)
                    act.copy(xlnT[:], XT).then_inc(xlnT_ready, 1)

            run_steps(act, step)

        @block.gpsimd
        def _(pool):
            pool.memset(pows[:, 0:1], -0.5)
            pool.memset(pows[:, 2:3], EPS)
            pool.memset(pows[:, 1:2], -1.0).then_inc(pows_ready, 1)
            pool.memset(rw[:], 0.5).then_inc(rw_half, 1)
            pool.wait_ge(pows_ready, 1)
            pool.wait_ge(rw_half, 1)
            pool.wait_ge(consts_in, 16)

            def inverse_root(t, mv, ve, rstd, mv_ready, ve_done, rstd_ready):
                wait(pool, mv_ready, t + 1)
                pool.tensor_tensor(ve[:], mv[:, 1:2], pows[:, 2:3], ALU.add).then_inc(ve_done, 1)
                wait(pool, ve_done, t + 1)
                pool.tensor_tensor(rstd[:], ve[:], pows[:, 0:1], ALU.pow).then_inc(rstd_ready, 1)

            def step(s, slot, k):
                m, n, p, q = s + 2, s + 1, s - 1, s - 2

                def weigh(f, t):
                    wait(pool, hu_ready[f], t + 1)
                    e0, e1 = part[f].start // FE, part[f].stop // FE
                    pool.tensor_tensor(hw[:, part[f]].rearrange("p (e f) -> p e f", f=FE),
                                       hu[:, part[f]].rearrange("p (e f) -> p e f", f=FE),
                                       rw[:, e0:e1].rearrange("p (e o) -> p e o", o=1).broadcast_to([P, e1 - e0, FE]),
                                       ALU.mult).then_inc(hw_ready[f], 1)

                if exists(k - 2):
                    weigh(1, q)
                if exists(k - 1):
                    inverse_root(p, mv2, ve2, rstd2, mv2_ready, ve2_done, rstd2_ready)
                if exists(k + 2) and not exists(k):
                    inverse_root(m, mv1, ve1, rstd1, mv1_ready, ve1_done, rstd1_ready)
                if exists(k + 1):
                    wait(pool, kT_ready, n + 1)
                    keys = kT[:].rearrange("p (b o k) -> p b o k", b=SEQS, o=1).broadcast_to([P, SEQS, 4, SEQ])
                    mask = head_mask.rearrange("p (o j u) -> p o j u", o=1, u=1).broadcast_to([P, SEQS, 4, SEQ])
                    pool.tensor_tensor(km[:, 1 - slot, :, :, :], keys, mask, ALU.mult).then_inc(km_ready, 1)
                if exists(k + 2) and exists(k):
                    inverse_root(m, mv1, ve1, rstd1, mv1_ready, ve1_done, rstd1_ready)
                if exists(k - 1):
                    wait_apart(pool, top_ready, p + 1, pows_ready)
                    pool.tensor_copy(top_atf[:], top_at[:])
                    wait_apart(pool, e21_ready, p + 1, pows_ready)
                    pool.tensor_scalar(den2[:], e21[:], 2.0, 2.0, ALU.mult, ALU.add).then_inc(den2_done, 1)
                    wait(pool, den2_done, p + 1)
                    pool.tensor_tensor(half_p[:, 0:1], den2[:], pows[:, 1:2], ALU.pow).then_inc(p1_done, 1)
                    wait(pool, p1_done, p + 1)
                    pool.tensor_tensor(half_p[:, 1:2], e21[:], half_p[:, 0:1], ALU.mult).then_inc(p2_done, 1)
                    wait_apart(pool, p2_done, p + 1, pows_ready)
                    for i in range(2):
                        pick_i = pool.tensor_scalar(pick[:, i, :], iota, top_atf[:, i:i + 1], half_p[:, i:i + 1],
                                                    ALU.is_equal, ALU.mult)
                    pick_i.then_inc(picked, 1)
                    wait(pool, picked, p + 1)
                    pool.tensor_tensor(rw[:, 0:EXPERTS], pick[:, 0, :], pick[:, 1, :], ALU.add).then_inc(rw_done, 1)
                    wait(pool, rw_done, p + 1)
                    weigh(0, p)

            run_steps(pool, step)

        @block.vector
        def _(dve):
            dve.memset(zeros[:], 0.0).then_inc(zeros_set, 1)
            dve.memset(vx[:], 0.0).then_inc(vx_zeroed, 1)
            dve.wait_ge(x_in, 16)

            def gated_part(f, p, k):
                wait(dve, th_ready[f], p + 1)
                dve.scalar_tensor_tensor(sg[:, part[f]], th[:, part[f]], 1.0, gu_banks(f, k)[0][:, 0:width[f]], ALU.add, ALU.mult) \
                   .then_inc(sg_done[f], 1)

            def up_part(f, p, k):
                if f == 1:
                    wait(dve, u_ready[f], p + 1)
                wait(dve, sg_done[f], p + 1)
                dve.tensor_tensor(hu[:, part[f]], sg[:, part[f]], gu_banks(f, k)[1][:, 0:width[f]], ALU.mult).then_inc(hu_ready[f], 1)

            def step(s, slot, k):
                m, a, p, q = s + 2, s, s - 1, s - 2

                def halves(c):
                    return slice(8 * c, 8 * c + 8)

                def maximum(c):
                    dve.tensor_reduce(row_max[:, halves(c)], ps_s[:, halves(c), :], AX.X, ALU.max).then_inc(max_done[c], 1)

                def shift(c):
                    wait(dve, max_done[c], a + 1)
                    dve.tensor_tensor(probs[:, slot, halves(c), :], ps_s[:, halves(c), :],
                                      row_max[:, halves(c)].rearrange("p (h o) -> p h o", o=1).broadcast_to([P, 8, SEQ]),
                                      ALU.subtract).then_inc(shifted[c], 1)

                if exists(k - 1):
                    if k == 1:
                        dve.wait_ge(gates_ready, 1)
                    wait(dve, y1_ready, p + 1)
                    dve.scalar_tensor_tensor(x1[:, 1 - slot, :], Y1, g_tanh[:, 0:1],
                                             x_all[:, bass.ds(p, 1), :].rearrange("p o d -> p (o d)"),
                                             ALU.mult, ALU.add).then_inc(x1_done, 1)
                if exists(k + 2):
                    if k == 0:
                        dve.wait_ge(x_next_in, 16)
                    elif k == 2:
                        dve.wait_ge(x_rest_in, 16)
                    x_m = x_all[:, bass.ds(m, 1), :].rearrange("p o d -> p (o d)")
                    dve.bn_stats(st1[:], x_m).then_inc(st1_done, 1)
                if exists(k - 1):
                    wait(dve, x1_done, p + 1)
                    dve.bn_stats(st2[:], x1[:, 1 - slot, :]).then_inc(st2_done, 1)
                if exists(k - 2):
                    up_part(1, q, k - 1)
                if exists(k - 1):
                    wait_apart(dve, st2_done, p + 1, gates_ready)
                    dve.bn_aggr(mv2[:], st2[:]).then_inc(mv2_ready, 1)
                if exists(k + 2):
                    if not exists(k - 1):
                        dve.wait_ge(st1_done, k + 3)
                    dve.bn_aggr(mv1[:], st1[:]).then_inc(mv1_ready, 1)
                if exists(k):
                    wait(dve, scores_ready, a + 1)
                    maximum(0)
                if exists(k):
                    shift(0)
                if exists(k - 1):
                    wait(dve, rstd2_ready, p + 1)
                    dve.tensor_scalar(x2ln[:], x1[:, 1 - slot, :], mv2[:, 0:1], rstd2[:, 0:1], ALU.subtract, ALU.mult) \
                       .then_inc(x2ln_ready, 1)
                if exists(k):
                    maximum(1)
                if exists(k - 1):
                    wait(dve, x2h_ready, p + 1)
                    dve.tensor_tensor(x2l[:], X2T, x2h[:].bitcast(F32), ALU.subtract).then_inc(x2l_ready, 1)
                if exists(k):
                    shift(1)
                if exists(k - 2):
                    wait(dve, y2_ready, q + 1)
                    if k - 2 >= 2:
                        wait(dve, stored[slot], (q - (k % 2)) * 8)
                    dve.scalar_tensor_tensor(outb[:, slot, :], Y2, g_tanh[:, 1:2], x1[:, slot, :],
                                             ALU.mult, ALU.add).then_inc(out_ready, 1)
                if exists(k + 2):
                    wait(dve, rstd1_ready, m + 1)
                    dve.tensor_scalar(xln[:, slot, :], x_m, mv1[:, 0:1], rstd1[:, 0:1], ALU.subtract, ALU.mult) \
                       .then_inc(xln_ready, 1)
                if exists(k - 1):
                    if k == 1:
                        dve.wait_ge(small_in, 32)
                    wait(dve, u_ready[0], p + 1)
                    dve.tensor_tensor(logits[:], ps_u[:, F0:F0 + EXPERTS], bias[:], ALU.add).then_inc(logits_done, 1)
                    wait_apart(dve, logits_done, p + 1, gates_ready)
                    dve.max(top[:], logits[:]).then_inc(top_done, 1)
                    wait_apart(dve, top_done, p + 1, gates_ready)
                    dve.max_index(top_at[:], top[:], logits[:]).then_inc(top_ready, 1)
                    gated_part(0, p, k)
                    up_part(0, p, k)
                if exists(k):
                    wait(dve, den_ready, a + 1)
                    dve.reciprocal(rden[:], D).then_inc(rden_done, 1)
                    wait(dve, pv_ready, a + 1)
                    wait(dve, rden_done, a + 1)
                    dve.tensor_tensor(oT[:], O, rden[:], ALU.mult).then_inc(oT_ready, 1)
                if exists(k - 1):
                    gated_part(1, p, k)
                if k == -1:
                    dve.wait_ge(ffn_in, 16)
                    dve.tensor_copy(we_hi[:], we[:, 0:E_D]).then_inc(we_hi_ready, 1)
                    dve.wait_ge(we_hi_ready, 1)
                    dve.tensor_tensor(we_lo[:], we[:, 0:E_D], we_hi[:].bitcast(F32), ALU.subtract).then_inc(we_lo_ready, 1)

            run_steps(dve, step)

        @block.tensor
        def _(pe):
            def scores(a, slot, half):
                for b in range(SEQS):
                    for quad in (half, half + 2):
                        rows = slice(32 * quad, 32 * quad + 32)
                        cols = slice(SEQ * b, SEQ * (b + 1))
                        mm = pe.matmul(ps_s[cols, 4 * quad:4 * quad + 4, :], qT[rows, slot, cols], km[rows, slot, b, :, :],
                                       start=True, stop=True, tile_position=(32 * quad, SEQ * b))
                return mm

            def gate_up(f, k):
                bank_g, bank_u = gu_banks(f, k)
                products = [(bank_g, g_cols[f], g_ready[f]), (bank_u, u_cols[f], u_ready[f])]
                order = products[::-1] if f == 0 else products
                for ps, cols, ready in order:
                    out_cols = ps[:, 0:cols.stop - cols.start]
                    pe.matmul(out_cols, x2h[:], we_lo[:, cols], start=True, stop=False)
                    pe.matmul(out_cols, x2h[:], we_hi[:, cols], start=False, stop=False)
                    pe.matmul(out_cols, x2l[:], we_hi[:, cols], start=False, stop=True).then_inc(ready, 1)

            def keep_warm(count, bank=ps_u):
                for _ in range(count):
                    pe.matmul(bank[:, 0:P], zeros[:], zeros[:], start=True, stop=True)

            def step(s, slot, k):
                m, n, a, p, q = s + 2, s + 1, s, s - 1, s - 2
                hT_parts = ((0, range(3)), (1, range(3, CHUNKS)))

                def transposed_products(f, chunks):
                    wait(pe, hw_ready[f], q + 1)
                    for i, c in enumerate(chunks):
                        mm = pe.transpose(ps_t[f][:, P * i:P * (i + 1)], hw[:, P * c:P * (c + 1)], ident)
                    mm.then_inc(hT_ready[f], 1)

                def down(f, chunks):
                    wait(pe, hT_copied[f], q + 1)
                    for c in chunks:
                        mm = pe.matmul(Y2, hT[:, c, :], we[:, E_D + P * c:E_D + P * (c + 1)],
                                       start=(c == 0), stop=(c == CHUNKS - 1))
                    return mm

                def transposed_probs(c):
                    wait(pe, probs_ready[c], a + 1)
                    for i in range(4):
                        h = 8 * c + 2 * i
                        mm = pe.transpose(ps_t[c][:, P * i:P * (i + 1)],
                                          probs[:, slot, h:h + 2, :].rearrange("p h k -> p (h k)"), ident)
                    mm.then_inc(pT_ready[c], 1)

                def transposed_norm():
                    if k == -2:
                        pe.wait_ge(consts_in, 16)
                        pe.wait_ge(attn_in, 16)
                    wait(pe, xln_ready, m + 1)
                    if exists(k + 1) and not exists(k - 1):
                        wait(pe, vx_ready, n + 1)
                    pe.transpose(XT, xln[:, slot, :], ident).then_inc(xT_ready, 1)

                if k == -2:
                    pe.wait_ge(zeros_set, 1)
                    keep_warm(WARM[0])
                if exists(k):
                    wait(pe, s_half_done, a + 1)
                    scores(a, slot, 1).then_inc(scores_ready, 1)
                if exists(k - 2):
                    transposed_products(*hT_parts[0])
                if exists(k + 1):
                    wait(pe, ctx_in[1 - slot], (n - ((k + 1) % 2)) * 8 + 16)
                    wait(pe, xlnT_ready, n + 1)
                    pe.matmul(K, wa[:, A_K:A_K + P], ctx[:, 1 - slot, :], start=True, stop=True)
                    for b in range(SEQS):
                        for h2 in range(2):
                            pe.matmul(V[SEQ * h2:SEQ * (h2 + 1), SEQ * b:SEQ * (b + 1)],
                                           ctx[:, 1 - slot, SEQ * b:SEQ * (b + 1)],
                                           wa[:, A_V + SEQ * h2:A_V + SEQ * (h2 + 1)],
                                           start=True, stop=True, tile_position=(0, SEQ * h2))
                    pe.matmul(Q, wa[:, A_Q:A_Q + P], xlnT[:], start=True, stop=True).then_inc(qkv_ready, 1)
                if k == -1:
                    keep_warm(WARM[1])
                    transposed_norm()
                    keep_warm(WARM[2])
                if k == 0:
                    keep_warm(WARM[3])
                if exists(k - 2):
                    transposed_products(*hT_parts[1])
                    if exists(k - 1):
                        wait(pe, x1_done, p + 1)
                    if k == last + 2:
                        keep_warm(WARM[7], ps_qkv)
                    down(*hT_parts[0])
                if k == 1:
                    keep_warm(WARM[5])
                if exists(k - 1):
                    if exists(k + 1):
                        wait(pe, vx_ready, n + 1)
                    wait(pe, x2ln_ready, p + 1)
                    pe.transpose(X2T, x2ln[:], ident).then_inc(x2T_ready, 1)
                if exists(k - 2):
                    down(*hT_parts[1]).then_inc(y2_ready, 1)
                if exists(k):
                    transposed_probs(0)
                if exists(k - 1):
                    if k == 1:
                        pe.wait_ge(we_lo_ready, 1)
                    wait(pe, x2l_ready, p + 1)
                    wait(pe, hu_ready[1], p)
                    gate_up(0, k)
                if k == 0:
                    keep_warm(WARM[4])
                if exists(k):
                    transposed_probs(1)
                if exists(k + 1):
                    wait(pe, shifted[1], n)
                    wait(pe, km_ready, n + 1)
                    wait(pe, qT_ready, n + 1)
                    scores(n, 1 - slot, 0).then_inc(s_half_done, 1)
                if exists(k):
                    wait(pe, pT_copied[0], a + 1)
                    wait(pe, pT_copied[1], a + 1)
                    for c in range(2):
                        for quad in range(QUADS):
                            mm = pe.matmul(D[32 * quad:32 * quad + 32, :], cst[:, C_ONES + 32 * c:C_ONES + 32 * (c + 1)],
                                           pT[:, 2 * quad + c, :], start=(c == 0), stop=(c == 1), tile_position=(0, 32 * quad))
                    mm.then_inc(den_ready, 1)
                if exists(k):
                    if exists(k - 2):
                        wait(pe, out_ready, q + 1)
                    for b in range(SEQS):
                        cols = slice(SEQ * b, SEQ * (b + 1))
                        for c in range(2):
                            for quad in range(QUADS):
                                pair = 2 * quad + c
                                mm = pe.matmul(O[32 * quad:32 * quad + 32, cols], v_window(slot, b, pair), pT[:, pair, cols],
                                               start=(c == 0), stop=(c == 1), tile_position=(0, 32 * quad))
                    mm.then_inc(pv_ready, 1)
                if exists(k - 1):
                    if k <= last:
                        wait(pe, hu_ready[0], p + 1)
                    gate_up(1, k)
                if k == last + 1:
                    keep_warm(WARM[6], ps_qkv)
                if exists(k + 2) and k != -1:
                    transposed_norm()
                if exists(k):
                    wait(pe, oT_ready, a + 1)
                    pe.matmul(Y1, oT[:], wa[:, A_O:A_O + P], start=True, stop=True).then_inc(y1_ready, 1)

            run_steps(pe, step)


def kernel(x, ctx_1024, g_xattn, g_ffn, L0_xattn_w_q, L0_xattn_w_k, L0_xattn_w_v, L0_xattn_w_o, L0_ffn_Wr,
           L0_ffn_Wg, L0_ffn_Wu, L0_ffn_Wd, L0_ffn_Sg, L0_ffn_Su, L0_ffn_Sd, L0_ffn_expert_bias):
    import numpy as np
    import concourse.bacc as bacc
    from concourse.bass_utils import run_bass_kernel_spmd

    shape = x.shape
    rows = shape[0] * shape[1]

    consts = np.zeros((P, C_END), np.float32)
    r = np.arange(P)
    consts[r, C_ID + r] = 1
    consts[r, C_MASK + r % 32 // HD] = 1
    consts[:, C_IOTA:C_IOTA + EXPERTS] = np.arange(EXPERTS)
    for c in range(2):
        for d in range(HD):
            consts[r, C_ONES + 32 * c + 16 * c + HD * (r // SEQ) + d] = 1

    wv = np.asarray(L0_xattn_w_v).reshape(PAIRS, 2, HD, P).transpose(1, 0, 2, 3).reshape(P, P)
    w_attn = np.concatenate([np.asarray(L0_xattn_w_q).T, np.asarray(L0_xattn_w_k).T, wv.T, np.asarray(L0_xattn_w_o).T], axis=1)

    def features(w, shared):
        return np.concatenate([np.asarray(w).transpose(1, 0, 2).reshape(P, EXPERTS * FE), np.asarray(shared)], axis=1)

    wg, wu = features(L0_ffn_Wg, L0_ffn_Sg), features(L0_ffn_Wu, L0_ffn_Su)
    wd = np.concatenate([np.asarray(L0_ffn_Wd).reshape(EXPERTS * FE, P), np.asarray(L0_ffn_Sd)], axis=0)
    wd = wd.reshape(CHUNKS, P, P).transpose(1, 0, 2).reshape(P, CHUNKS * P)
    w_ffn = np.concatenate([wg[:, :F0], wu[:, :F0], np.asarray(L0_ffn_Wr), wg[:, F0:], wu[:, F0:], wd], axis=1)

    arrays = {
        "x": np.asarray(x).reshape(rows, P),
        "ctxT": np.asarray(ctx_1024).reshape(rows, P).T,
        "gates": np.concatenate([np.asarray(g_xattn), np.asarray(g_ffn)]),
        "consts": consts,
        "w_attn": w_attn,
        "w_ffn": w_ffn,
        "expert_bias": np.asarray(L0_ffn_expert_bias),
    }
    arrays = {k: np.ascontiguousarray(v) for k, v in arrays.items()}
    nc = bacc.Bacc("TRN2", target_bir_lowering=False, num_devices=1)
    args = [nc.dram_tensor(k, v.shape, mybir.dt.from_np(v.dtype), kind="ExternalInput").ap() for k, v in arrays.items()]
    out = nc.dram_tensor("out", (rows, P), F32, kind="ExternalOutput").ap()
    block_kernel(nc, *args, out)
    got = run_bass_kernel_spmd(nc, [arrays], core_ids=[0])
    return got.results[0]["out"].reshape(shape)
```
